# Optimizing a Trainium2 kernel written in Bass

```python
import numpy as np
import jax
import jax.numpy as jnp

def _softmax(x, axis=-1):
    return jax.nn.softmax(x, axis=axis)

def _gelu(x):
    return jax.nn.gelu(x, approximate=True)

def _silu(x):
    return jax.nn.silu(x)

def _sigmoid(x):
    return jax.nn.sigmoid(x)

def _layernorm(x, axis=-1, eps=1e-05):
    m = jnp.mean(x, axis=axis, keepdims=True)
    v = jnp.var(x, axis=axis, keepdims=True)
    return (x - m) / jnp.sqrt(v + eps)

def _scatter_add(tgt, idx, src, axis=0):
    return tgt.at[idx].add(src)

def _segment_sum(src, seg, n):
    return jax.ops.segment_sum(src, seg, n)
kernel_name = 'mk_dlrm_tower_d1_rec_r8_e68ca1'

def setup_inputs(seed: int=0):
    np.random.seed(seed)
    _w = jnp.asarray

    def _rec_inputs():
        import jax
        import jax.numpy as jnp
        _tk = jax.random.key(seed)
        ids = jnp.stack([jax.random.randint(jax.random.fold_in(_tk, 200 + f), (512,), 0, v, jnp.int32) for f, v in enumerate([1250, 12500, 125000, 12500, 1250, 1000, 12500, 12500, 1250, 12500, 1000, 12500, 12500, 1250, 1250, 1250, 1250, 1250, 1250, 1250, 1250, 1250, 1250, 1250, 1250, 12500])], axis=1)
        tbl_0 = 0.05 * jax.random.normal(jax.random.fold_in(_tk, 500 + 0), (1250, 128), jnp.float32)
        tbl_1 = 0.05 * jax.random.normal(jax.random.fold_in(_tk, 500 + 1), (12500, 128), jnp.float32)
        tbl_2 = 0.05 * jax.random.normal(jax.random.fold_in(_tk, 500 + 2), (125000, 128), jnp.float32)
        tbl_3 = 0.05 * jax.random.normal(jax.random.fold_in(_tk, 500 + 3), (12500, 128), jnp.float32)
        tbl_4 = 0.05 * jax.random.normal(jax.random.fold_in(_tk, 500 + 4), (1250, 128), jnp.float32)
        tbl_5 = 0.05 * jax.random.normal(jax.random.fold_in(_tk, 500 + 5), (1000, 128), jnp.float32)
        tbl_6 = 0.05 * jax.random.normal(jax.random.fold_in(_tk, 500 + 6), (12500, 128), jnp.float32)
        tbl_7 = 0.05 * jax.random.normal(jax.random.fold_in(_tk, 500 + 7), (12500, 128), jnp.float32)
        tbl_8 = 0.05 * jax.random.normal(jax.random.fold_in(_tk, 500 + 8), (1250, 128), jnp.float32)
        tbl_9 = 0.05 * jax.random.normal(jax.random.fold_in(_tk, 500 + 9), (12500, 128), jnp.float32)
        tbl_10 = 0.05 * jax.random.normal(jax.random.fold_in(_tk, 500 + 10), (1000, 128), jnp.float32)
        tbl_11 = 0.05 * jax.random.normal(jax.random.fold_in(_tk, 500 + 11), (12500, 128), jnp.float32)
        tbl_12 = 0.05 * jax.random.normal(jax.random.fold_in(_tk, 500 + 12), (12500, 128), jnp.float32)
        tbl_13 = 0.05 * jax.random.normal(jax.random.fold_in(_tk, 500 + 13), (1250, 128), jnp.float32)
        tbl_14 = 0.05 * jax.random.normal(jax.random.fold_in(_tk, 500 + 14), (1250, 128), jnp.float32)
        tbl_15 = 0.05 * jax.random.normal(jax.random.fold_in(_tk, 500 + 15), (1250, 128), jnp.float32)
        tbl_16 = 0.05 * jax.random.normal(jax.random.fold_in(_tk, 500 + 16), (1250, 128), jnp.float32)
        tbl_17 = 0.05 * jax.random.normal(jax.random.fold_in(_tk, 500 + 17), (1250, 128), jnp.float32)
        tbl_18 = 0.05 * jax.random.normal(jax.random.fold_in(_tk, 500 + 18), (1250, 128), jnp.float32)
        tbl_19 = 0.05 * jax.random.normal(jax.random.fold_in(_tk, 500 + 19), (1250, 128), jnp.float32)
        tbl_20 = 0.05 * jax.random.normal(jax.random.fold_in(_tk, 500 + 20), (1250, 128), jnp.float32)
        tbl_21 = 0.05 * jax.random.normal(jax.random.fold_in(_tk, 500 + 21), (1250, 128), jnp.float32)
        tbl_22 = 0.05 * jax.random.normal(jax.random.fold_in(_tk, 500 + 22), (1250, 128), jnp.float32)
        tbl_23 = 0.05 * jax.random.normal(jax.random.fold_in(_tk, 500 + 23), (1250, 128), jnp.float32)
        tbl_24 = 0.05 * jax.random.normal(jax.random.fold_in(_tk, 500 + 24), (1250, 128), jnp.float32)
        tbl_25 = 0.05 * jax.random.normal(jax.random.fold_in(_tk, 500 + 25), (12500, 128), jnp.float32)
        _rk = jax.random.fold_in(_tk, 7)
        r_dense_features = -0.000520686 + 1.00062 * jax.random.normal(jax.random.fold_in(_rk, 101), (512, 128), jnp.float32)
        W_top1 = 0.0405887 * jax.random.normal(jax.random.fold_in(_tk, 801), (607, 512), jnp.float32)
        W_top2 = 0.0441942 * jax.random.normal(jax.random.fold_in(_tk, 802), (512, 256), jnp.float32)
        W_top3 = 0.0625 * jax.random.normal(jax.random.fold_in(_tk, 803), (256, 1), jnp.float32)
        b_top1 = jnp.zeros((512,), jnp.float32)
        b_top2 = jnp.zeros((256,), jnp.float32)
        return (r_dense_features, ids, tbl_0, tbl_1, tbl_2, tbl_3, tbl_4, tbl_5, tbl_6, tbl_7, tbl_8, tbl_9, tbl_10, tbl_11, tbl_12, tbl_13, tbl_14, tbl_15, tbl_16, tbl_17, tbl_18, tbl_19, tbl_20, tbl_21, tbl_22, tbl_23, tbl_24, tbl_25, W_top1, b_top1, W_top2, b_top2, W_top3)
    r_dense_features, ids, tbl_0, tbl_1, tbl_2, tbl_3, tbl_4, tbl_5, tbl_6, tbl_7, tbl_8, tbl_9, tbl_10, tbl_11, tbl_12, tbl_13, tbl_14, tbl_15, tbl_16, tbl_17, tbl_18, tbl_19, tbl_20, tbl_21, tbl_22, tbl_23, tbl_24, tbl_25, W_top1, b_top1, W_top2, b_top2, W_top3 = _rec_inputs()

    def _L0_rec_setup():
        import jax, jax.numpy as jnp
        import numpy as np
        F = 26
        N = F + 1
        _TRIU_I, _TRIU_J = np.triu_indices(N, k=1)
        key = jax.random.key(seed)
        k1, k2 = jax.random.split(key)
        B, D = (2048, 128)
        dense_features = jax.random.normal(k1, (B, D), dtype=jnp.float32)
        sparse_features = jax.random.normal(k2, (B, F, D), dtype=jnp.float32)
        return {'dense_features': dense_features, 'sparse_features': sparse_features}
    _L0_rec_all = _L0_rec_setup()
    _L0_rec_in = {k: v for k, v in _L0_rec_all.items() if k in ()}
    del _L0_rec_all
    return {'r_dense_features': r_dense_features, 'ids': ids, 'tbl_0': tbl_0, 'tbl_1': tbl_1, 'tbl_2': tbl_2, 'tbl_3': tbl_3, 'tbl_4': tbl_4, 'tbl_5': tbl_5, 'tbl_6': tbl_6, 'tbl_7': tbl_7, 'tbl_8': tbl_8, 'tbl_9': tbl_9, 'tbl_10': tbl_10, 'tbl_11': tbl_11, 'tbl_12': tbl_12, 'tbl_13': tbl_13, 'tbl_14': tbl_14, 'tbl_15': tbl_15, 'tbl_16': tbl_16, 'tbl_17': tbl_17, 'tbl_18': tbl_18, 'tbl_19': tbl_19, 'tbl_20': tbl_20, 'tbl_21': tbl_21, 'tbl_22': tbl_22, 'tbl_23': tbl_23, 'tbl_24': tbl_24, 'tbl_25': tbl_25, 'W_top1': W_top1, 'b_top1': b_top1, 'W_top2': W_top2, 'b_top2': b_top2, 'W_top3': W_top3}

def reference(r_dense_features, ids, tbl_0, tbl_1, tbl_2, tbl_3, tbl_4, tbl_5, tbl_6, tbl_7, tbl_8, tbl_9, tbl_10, tbl_11, tbl_12, tbl_13, tbl_14, tbl_15, tbl_16, tbl_17, tbl_18, tbl_19, tbl_20, tbl_21, tbl_22, tbl_23, tbl_24, tbl_25, W_top1, b_top1, W_top2, b_top2, W_top3):
    import jax
    import jax.numpy as jnp

    def _L0_rec_ref(dense_features, sparse_features):
        import jax, jax.numpy as jnp
        import numpy as np
        F = 26
        N = F + 1
        _TRIU_I, _TRIU_J = np.triu_indices(N, k=1)
        combined = jnp.concatenate([dense_features[:, None, :], sparse_features], axis=1)
        interactions = jnp.einsum('bnd,bmd->bnm', combined, combined)
        interactions_flat = interactions[:, _TRIU_I, _TRIU_J]
        return jnp.concatenate([dense_features, interactions_flat], axis=1)
    e = jnp.stack([tbl_0[ids[:, 0]], tbl_1[ids[:, 1]], tbl_2[ids[:, 2]], tbl_3[ids[:, 3]], tbl_4[ids[:, 4]], tbl_5[ids[:, 5]], tbl_6[ids[:, 6]], tbl_7[ids[:, 7]], tbl_8[ids[:, 8]], tbl_9[ids[:, 9]], tbl_10[ids[:, 10]], tbl_11[ids[:, 11]], tbl_12[ids[:, 12]], tbl_13[ids[:, 13]], tbl_14[ids[:, 14]], tbl_15[ids[:, 15]], tbl_16[ids[:, 16]], tbl_17[ids[:, 17]], tbl_18[ids[:, 18]], tbl_19[ids[:, 19]], tbl_20[ids[:, 20]], tbl_21[ids[:, 21]], tbl_22[ids[:, 22]], tbl_23[ids[:, 23]], tbl_24[ids[:, 24]], tbl_25[ids[:, 25]]], axis=1)
    z = _L0_rec_ref(r_dense_features, e)
    z = z.reshape(z.shape[0], -1)
    h = jnp.concatenate([z, r_dense_features], axis=1)
    h = jnp.maximum(h @ W_top1 + b_top1, 0.0)
    h = jnp.maximum(h @ W_top2 + b_top2, 0.0)
    y = h @ W_top3
    return y

_drawn_inputs = setup_inputs


def setup_inputs(seed=0):
    import zlib

    import numpy as np

    out = dict(_drawn_inputs(seed))
    spreads = {'b_top1': (0.0, 0.1), 'b_top2': (0.0, 0.1)}
    factors = {}
    for name, (base, spread) in spreads.items():
        noise = np.random.default_rng([zlib.crc32(name.encode()), seed]).standard_normal(out[name].shape)
        drawn = base * np.exp(spread * noise) if base else spread * noise
        out[name] = jnp.asarray(drawn.astype(out[name].dtype))
    for name, factor in factors.items():
        out[name] = (out[name] * factor).astype(out[name].dtype)
    return out
```

```python
import numpy as np
import concourse.bass as bass
from concourse import mybir
from contextlib import ExitStack

FP32 = mybir.dt.float32
INT32 = mybir.dt.int32
ALU = mybir.AluOpType
ACT = mybir.ActivationFunctionType

P = 128
D = 128
TABLES = 26
FEATS = TABLES + 1
SLOT = 32
BATCH = 512
TILES = BATCH // P
H1, H2 = 512, 256
K2 = H1 // P

GROUP = 4
GROUPS = -(-TABLES // GROUP)
FIRST_HALF = 3
SPLIT = FIRST_HALF * GROUP

QUAD = P // SLOT
GRAMS = P // QUAD
PER_BANK = 4
CHUNK_BANKS = 2
CHUNK = PER_BANK * CHUNK_BANKS
CHUNKS = GRAMS // CHUNK

STARS = FEATS - 1
STEPS = -(-STARS // QUAD)


def groups_of(j):
    return min(GROUP, TABLES - GROUP * j)


def build(nc, ids, tables, dense, w1, b1, w2, b2, w3, out):
    ctx = ExitStack()
    with ctx:
        def sb(name, shape, dt=FP32):
            return ctx.enter_context(nc.sbuf_tensor(name, shape, dt))

        def ps(name, shape):
            return ctx.enter_context(nc.psum_tensor(name, shape, FP32))

        def sem(name):
            return ctx.enter_context(nc.semaphore(name))

        ids_half = [sb("ids_first", [P, SPLIT], INT32), sb("ids_second", [P, TABLES - SPLIT], INT32)]
        rows = sb("rows", [P, TABLES, D])
        dense_rows = sb("dense_rows", [P, TILES, D])
        ident = sb("ident", [P, P])
        denseT = sb("denseT", [D, TILES, P])
        denseT_now = sb("denseT_now", [D, P])
        featT = sb("featT", [D, P, SLOT])
        dots = sb("dots", [P, STEPS, P])
        w_dense = sb("w_dense", [P, 2, H1])
        w_dsum = sb("w_dsum", [P, H1])
        w_dots = sb("w_dots", [P, STEPS, H1])
        w_mid = sb("w_mid", [P, K2, H2])
        b1_col = sb("b1_col", [P, K2])
        b2_all = sb("b2_all", [P, H2])
        w3_all = sb("w3_all", [P, H2])
        h1 = sb("h1", [P, H1])
        h1T = sb("h1T", [P, K2, P])
        h2 = sb("h2", [P, H2])
        h2w = sb("h2w", [P, H2])
        y_now = sb("y_now", [P, 1])
        y_all = sb("y_all", [P, TILES])

        turned = [ps("turned_even", [P, GROUP, P]), ps("turned_odd", [P, GROUP, P])]
        gram = [ps("gram_even", [P, CHUNK_BANKS, P * PER_BANK]), ps("gram_odd", [P, CHUNK_BANKS, P * PER_BANK])]
        layer = ps("layer", [P, H1])
        h1_turned = ps("h1_turned", [P, K2, P])

        ids_ready = [sem("ids_ready_first"), sem("ids_ready_second")]
        dense_loaded = sem("dense_loaded")
        gathered = [sem(f"gathered_{j}") for j in range(GROUPS)]
        ident_zero = sem("ident_zero")
        ident_ready = sem("ident_ready")
        w_zeroed = sem("w_zeroed")
        wd_loaded = sem("wd_loaded")
        wdots_loaded = sem("wdots_loaded")
        wmid_loaded = sem("wmid_loaded")
        small_loaded = sem("small_loaded")
        wsum_ready = sem("wsum_ready")
        dense_turned = sem("dense_turned")
        denseT_ready = sem("denseT_ready")
        tile_dense = sem("tile_dense")
        pads_zeroed = sem("pads_zeroed")
        turned_done = sem("turned_done")
        feat_vec = sem("feat_vec")
        feat_act = sem("feat_act")
        gram_done = sem("gram_done")
        dots_vec = sem("dots_vec")
        dots_act = sem("dots_act")
        l1_done = sem("l1_done")
        h1_ready = sem("h1_ready")
        h1_turned_done = sem("h1_turned_done")
        h1T_ready = sem("h1T_ready")
        l2_done = sem("l2_done")
        h2_ready = sem("h2_ready")
        y_ready = sem("y_ready")
        y_stored = sem("y_stored")
        out_written = sem("out_written")

        ids_tiled = ids.rearrange("(p t) f -> p t f", t=TILES)
        ids_src = [ids_tiled[:, :, 0:SPLIT], ids_tiled[:, :, SPLIT:TABLES]]
        half_groups = [range(0, FIRST_HALF), range(FIRST_HALF, GROUPS)]
        EVENS, ODDS = (GROUPS + 1) // 2, GROUPS // 2

        featT_by_feat = featT[:, :, :].rearrange("d b n -> d n b")
        dots_cols = dots[:, :, :].rearrange("p k (c a b s) -> p s c k a b", s=QUAD, c=CHUNKS, a=CHUNK_BANKS)

        def spread(copy, s, c):
            src = gram[c % 2][SLOT * s:SLOT * (s + 1), :, 0:PER_BANK * QUAD * FEATS].rearrange(
                "n a (b e m) -> n e m a b", b=PER_BANK, e=QUAD)
            for r in range(QUAD):
                ks = len(range(r, STARS, QUAD))
                last = copy(dots_cols[SLOT * r:SLOT * (r + 1), s, c, 0:ks],
                            src[:, s, r:r + QUAD * (ks - 1) + 1:QUAD])
            return last

        block = ctx.enter_context(nc.Block())

        @block.sync
        def _(sp):
            for h in range(2):
                sp.dma_start(ids_half[h][:, :], ids_src[h][:, 0, :]).then_inc(ids_ready[h], 16)
            sp.dma_start(dense_rows[:, :, :], dense.rearrange("(p t) d -> p t d", t=TILES)).then_inc(dense_loaded, 16)
            sp.dma_start(w_dense[:, 0, :], w1[0:D, :]).then_inc(wd_loaded, 16)
            sp.dma_start(w_dense[:, 1, :], w1[w1.shape[0] - D:, :]).then_inc(wd_loaded, 16)
            sp.wait_ge(w_zeroed, 1)
            row = D
            for m in range(STARS):
                k, r, n = m // QUAD, m % QUAD, FEATS - 1 - m
                sp.dma_start(w_dots[SLOT * r + m + 1:SLOT * r + FEATS, k, :], w1[row:row + n, :]).then_inc(
                    wdots_loaded, 16)
                row += n
            sp.dma_start(b1_col[:, :], b1.rearrange("(c p o) -> p c o", p=P, o=1),
                         allow_slow_non_contiguous=True).then_inc(small_loaded, 16)
            sp.dma_start(b2_all[:, :], b2.rearrange("(o n) -> o n", o=1).broadcast_to([P, H2])).then_inc(small_loaded, 16)
            sp.dma_start(w3_all[:, :], w3.rearrange("n o -> o n").broadcast_to([P, H2])).then_inc(small_loaded, 16)
            sp.dma_start(w_mid[:, :, :], w2.rearrange("(c p) n -> p c n", p=P)).then_inc(wmid_loaded, 16)
            with sp.Fori(1, TILES) as t:
                for h in range(2):
                    sp.wait_ge(w_zeroed, 1)
                    for j in half_groups[h]:
                        sp.wait_ge(gathered[j], 16 * groups_of(j) * t)
                    sp.dma_start(ids_half[h][:, :], ids_src[h][:, bass.ds(t, 1), :]).then_inc(ids_ready[h], 16)
            sp.wait_ge(y_stored, TILES)
            sp.dma_start(out.rearrange("(p t) o -> p (t o)", t=TILES), y_all[:, :]).then_inc(out_written, 16)
            sp.wait_ge(out_written, 16)

        @block.gpsimd
        def _(pool):
            nc.gpsimd.memset(ident[:, :], 0.0).then_inc(ident_zero, 1)
            pool.wait_ge(ident_zero, 1)
            nc.gpsimd.affine_select(out=ident[:, :], in_=ident[:, :], compare_op=ALU.not_equal, fill=1.0, base=0,
                                    pattern=[[-1, P]], channel_multiplier=1).then_inc(ident_ready, 1)

            def gather(j):
                h = int(j >= FIRST_HALF)
                for f in range(GROUP * j, GROUP * j + groups_of(j)):
                    col = f - h * SPLIT
                    pool.indirect_dma_start(rows[:, f, :], None, tables[f],
                                            bass.IndirectOffsetOnAxis(ap=ids_half[h][:, col:col + 1], axis=0)
                                            ).then_inc(gathered[j], 16)

            for j in range(GROUPS):
                if j in (0, FIRST_HALF):
                    pool.wait_ge(ids_ready[int(j > 0)], 16)
                gather(j)
            groups_read = pool.alloc_register("groups_read")
            pool.reg_mov(groups_read, 1)
            with pool.Fori(1, TILES) as t:
                for j in range(GROUPS):
                    if j in (0, FIRST_HALF):
                        pool.wait_ge(ids_ready[int(j > 0)], 16 * (t + 1))
                    pool.wait_ge(turned_done, groups_read)
                    pool.reg_add(groups_read, groups_read, 1)
                    gather(j)

        @block.tensor
        def _(pe):
            pe.wait_ge(dense_loaded, 16)
            pe.wait_ge(ident_ready, 1)
            for t in range(TILES):
                last = nc.tensor.transpose(turned[0][:, t, :], dense_rows[:, t, :], ident[:, :])
            last.then_inc(dense_turned, 1)
            pe.wait_ge(denseT_ready, 1)
            pe.wait_ge(pads_zeroed, 1)
            pe.wait_ge(wsum_ready, 1)
            pe.wait_ge(wdots_loaded, 16 * STARS)
            pe.wait_ge(wmid_loaded, 16)
            def tile(t, first):
                for j in range(GROUPS):
                    pe.wait_ge(gathered[j], 16 * groups_of(j) * (t + 1))
                    if j % 2 == 0 and not (first and j == 0):
                        pe.wait_ge(feat_vec, EVENS * t + j // 2)
                    if j % 2 == 1 and not (first and j == 1):
                        pe.wait_ge(feat_act, ODDS * t + j // 2)
                    for i in range(groups_of(j)):
                        last = nc.tensor.transpose(turned[j % 2][:, i, :], rows[:, GROUP * j + i, :], ident[:, :])
                    last.then_inc(turned_done, 1)
                pe.wait_ge(tile_dense, t + 1)
                pe.wait_ge(feat_vec, EVENS * (t + 1))
                pe.wait_ge(feat_act, ODDS * (t + 1))
                for c in range(CHUNKS):
                    if not (first and c < 2):
                        done = CHUNKS * t + max(c - 1, 0)
                        pe.wait_ge(dots_vec, done)
                        pe.wait_ge(dots_act, done)
                    for a in range(CHUNK_BANKS):
                        for b in range(PER_BANK):
                            g = CHUNK * c + PER_BANK * a + b
                            cols = QUAD * FEATS
                            last = nc.tensor.matmul(
                                gram[c % 2][:, a, cols * b:cols * (b + 1)].rearrange("p (s n) -> p s n", s=QUAD),
                                featT[:, QUAD * g:QUAD * (g + 1), :], featT[:, QUAD * g:QUAD * (g + 1), 0:FEATS], start=True, stop=True)
                    last.then_inc(gram_done, 1)
                nc.tensor.matmul(layer[:, :], denseT_now[:, :], w_dsum[:, :], start=True, stop=False)
                pe.wait_ge(dots_vec, CHUNKS * (t + 1))
                pe.wait_ge(dots_act, CHUNKS * (t + 1))
                for k in range(STEPS):
                    kp = SLOT * len(range(QUAD * k, min(QUAD * (k + 1), STARS)))
                    last = nc.tensor.matmul(layer[:, :], dots[0:kp, k, :], w_dots[0:kp, k, :], start=False,
                                            stop=k == STEPS - 1)
                last.then_inc(l1_done, 1)
                pe.wait_ge(h1_ready, t + 1)
                for k in range(K2):
                    last = nc.tensor.transpose(h1_turned[:, k, :], h1[:, P * k:P * (k + 1)], ident[:, :])
                last.then_inc(h1_turned_done, 1)
                pe.wait_ge(h1T_ready, t + 1)
                for k in range(K2):
                    last = nc.tensor.matmul(layer[:, 0:H2], h1T[:, k, :], w_mid[:, k, :], start=k == 0,
                                            stop=k == K2 - 1)
                last.then_inc(l2_done, 1)

            tile(0, True)
            with pe.Fori(1, TILES) as t:
                tile(t, False)

        @block.scalar
        def _(act):
            act.wait_ge(small_loaded, 16 * 3)
            act.wait_ge(pads_zeroed, 1)
            def tile(t, first):
                if not first:
                    act.wait_ge(gram_done, CHUNKS * t)
                for j in range(1, GROUPS, 2):
                    act.wait_ge(turned_done, GROUPS * t + j + 1)
                    n, f = groups_of(j), 1 + GROUP * j
                    nc.scalar.copy(featT_by_feat[:, f:f + n], turned[1][:, 0:n, :]).then_inc(feat_act, 1)
                if not first:
                    act.wait_ge(l1_done, t)
                for c in range(CHUNKS):
                    act.wait_ge(gram_done, CHUNKS * t + c + 1)
                    spread(nc.scalar.copy, 2, c)
                    spread(nc.scalar.copy, 3, c).then_inc(dots_act, 1)
                act.wait_ge(h1_turned_done, t + 1)
                if not first:
                    act.wait_ge(l2_done, t)
                for k in range(K2):
                    last = nc.scalar.activation(h1T[:, k, :], h1_turned[:, k, :], ACT.Relu, bias=b1_col[:, k:k + 1])
                last.then_inc(h1T_ready, 1)

            tile(0, True)
            with act.Fori(1, TILES) as t:
                tile(t, False)

        @block.vector
        def _(dve):
            nc.vector.memset(w_dots[:, :, :], 0.0).then_inc(w_zeroed, 1)
            nc.vector.memset(featT[:, :, FEATS:SLOT], 0.0).then_inc(pads_zeroed, 1)
            dve.wait_ge(dense_turned, 1)
            nc.vector.tensor_copy(denseT[:, :, :], turned[0][:, :, :]).then_inc(denseT_ready, 1)
            dve.wait_ge(wd_loaded, 32)
            nc.vector.tensor_add(w_dsum[:, :], w_dense[:, 0, :], w_dense[:, 1, :]).then_inc(wsum_ready, 1)
            dve.wait_ge(small_loaded, 16 * 3)
            dve.wait_ge(denseT_ready, 1)
            def tile(t, first):
                if not first:
                    dve.wait_ge(gram_done, CHUNKS * t)
                if not first:
                    dve.wait_ge(l1_done, t)
                nc.vector.tensor_copy(denseT_now[:, :], denseT[:, bass.ds(t, 1), :].rearrange("d t b -> d (t b)"))
                nc.vector.tensor_copy(featT[:, :, 0], denseT[:, bass.ds(t, 1), :].rearrange("d t b -> d (t b)")
                                      ).then_inc(tile_dense, 1)
                for j in range(0, GROUPS, 2):
                    dve.wait_ge(turned_done, GROUPS * t + j + 1)
                    n, f = groups_of(j), 1 + GROUP * j
                    nc.vector.tensor_copy(featT_by_feat[:, f:f + n], turned[0][:, 0:n, :]).then_inc(feat_vec, 1)
                for c in range(CHUNKS):
                    dve.wait_ge(gram_done, CHUNKS * t + c + 1)
                    spread(nc.vector.tensor_copy, 0, c)
                    spread(nc.vector.tensor_copy, 1, c).then_inc(dots_vec, 1)
                dve.wait_ge(l1_done, t + 1)
                nc.vector.tensor_copy(h1[:, :], layer[:, :]).then_inc(h1_ready, 1)
                dve.wait_ge(l2_done, t + 1)
                nc.vector.tensor_add(h2[:, :], layer[:, 0:H2], b2_all[:, :]).then_inc(h2_ready, 1)
                dve.wait_ge(h2_ready, t + 1)
                nc.vector.scalar_tensor_tensor(h2w[:, :], h2[:, :], 0.0, w3_all[:, :], op0=ALU.max, op1=ALU.mult,
                                               accum_out=y_now[:, :]).then_inc(y_ready, 1)
                dve.wait_ge(y_ready, t + 1)
                nc.vector.tensor_copy(y_all[:, bass.ds(t, 1)], y_now[:, :]).then_inc(y_stored, 1)

            tile(0, True)
            with dve.Fori(1, TILES) as t:
                tile(t, False)


def kernel(**inputs):
    import concourse.bacc as bacc
    from concourse.bass_utils import run_bass_kernel_spmd

    nc = bacc.Bacc("TRN2", target_bir_lowering=False, num_devices=1)
    arrays = {}

    def given(name):
        a = np.ascontiguousarray(inputs[name])
        arrays[f"in_{name}"] = a
        return nc.dram_tensor(f"in_{name}", a.shape, mybir.dt.from_np(a.dtype), kind="ExternalInput").ap()

    ids = given("ids")
    tables = [given(f"tbl_{f}") for f in range(TABLES)]
    dense, w1, b1, w2, b2, w3 = (given(n) for n in ("r_dense_features", "W_top1", "b_top1", "W_top2", "b_top2",
                                                    "W_top3"))
    out = nc.dram_tensor("out", (BATCH, 1), FP32, kind="ExternalOutput").ap()
    build(nc, ids, tables, dense, w1, b1, w2, b2, w3, out)
    return run_bass_kernel_spmd(nc, [arrays], core_ids=[0]).results[0]["out"]
```

```python
import numpy as np
import concourse.bass as bass
from concourse import mybir
from contextlib import ExitStack

FP32 = mybir.dt.float32
FP32R = mybir.dt.float32r
INT32 = mybir.dt.int32
ALU = mybir.AluOpType
ACT = mybir.ActivationFunctionType

P = 128
D = 128
TABLES = 26
FEATS = TABLES + 1
SLOT = 32
BATCH = 512
TILES = BATCH // P
H1, H2 = 512, 256
K2 = H1 // P

HOT_FIRST, HOT = 20, 5
HOT_ROWS = 1250
ROW_BLOCKS = 10
HOT_P = HOT_ROWS // ROW_BLOCKS
HOT_CUT = 112
ONES = 4

GATHERED = [f for f in range(TABLES) if not HOT_FIRST <= f < HOT_FIRST + HOT]
GROUP = 4
MEMBERS = [GATHERED[i:i + GROUP] for i in range(0, len(GATHERED), GROUP)]
GROUPS = len(MEMBERS)
FIRST_HALF = GROUPS // 2
SPLIT = MEMBERS[FIRST_HALF][0]

QUAD = P // SLOT
GRAMS = P // QUAD
PER_BANK = 4
CHUNK_BANKS = 2
CHUNK = PER_BANK * CHUNK_BANKS
CHUNKS = GRAMS // CHUNK

STARS = FEATS - 1
STEPS = -(-STARS // QUAD)


def runs(members):
    out = []
    for i, f in enumerate(members):
        if out and f == out[-1][1] + out[-1][2]:
            out[-1][2] += 1
        else:
            out.append([i, f, 1])
    return out


def build(nc, ids, hot_ids, tables, dense, w1, b1, w2, b2, w3, out):
    ctx = ExitStack()
    with ctx:
        def sb(name, shape, dt=FP32):
            return ctx.enter_context(nc.sbuf_tensor(name, shape, dt))

        def ps(name, shape):
            return ctx.enter_context(nc.psum_tensor(name, shape, FP32))

        def sem(name):
            return ctx.enter_context(nc.semaphore(name))

        ids_half = [sb("ids_first", [P, SPLIT], INT32), sb("ids_second", [P, TABLES - SPLIT], INT32)]
        rows = sb("rows", [P, TABLES, D])
        dense_rows = sb("dense_rows", [P, TILES, D])
        hot_ids_all = sb("hot_ids_all", [HOT_P, HOT, BATCH], INT32)
        hot_rows = sb("hot_rows", [HOT_P, HOT, ROW_BLOCKS, D])
        hot_hi = [sb(f"hot_hi_{i}", [HOT_P, ROW_BLOCKS, D], FP32R) for i in range(2)]
        hot_lo = [sb(f"hot_lo_{i}", [HOT_P, ROW_BLOCKS, D], FP32R) for i in range(2)]
        onehot = [sb(f"onehot_{i}", [HOT_P, BATCH], FP32R) for i in range(ONES)]
        row_no_int = sb("row_no_int", [HOT_P, ROW_BLOCKS], INT32)
        row_no = sb("row_no", [HOT_P, ROW_BLOCKS])
        hotT = sb("hotT", [D, HOT, TILES, P])
        ident = sb("ident", [P, P])
        denseT = sb("denseT", [D, TILES, P])
        denseT_now = sb("denseT_now", [D, P])
        featT = sb("featT", [D, P, SLOT])
        dots = sb("dots", [P, STEPS, P])
        w_dense = sb("w_dense", [P, 2, H1])
        w_dsum = sb("w_dsum", [P, H1])
        w_dots = sb("w_dots", [P, STEPS, H1])
        w_mid = sb("w_mid", [P, K2, H2])
        b1_col = sb("b1_col", [P, K2])
        b2_all = sb("b2_all", [P, H2])
        w3_all = sb("w3_all", [P, H2])
        h1 = sb("h1", [P, H1])
        h1T = sb("h1T", [P, K2, P])
        h2 = sb("h2", [P, H2])
        h2w = sb("h2w", [P, H2])
        y_now = sb("y_now", [P, 1])
        y_all = sb("y_all", [P, TILES])

        turned = [ps("turned_even", [P, GROUP, P]), ps("turned_odd", [P, GROUP, P])]
        gram = [ps("gram_even", [P, CHUNK_BANKS, P * PER_BANK]), ps("gram_odd", [P, CHUNK_BANKS, P * PER_BANK])]
        layer = ps("layer", [P, H1])
        h1_turned = ps("h1_turned", [P, K2, P])
        hot_sum = [layer[:, :], h1_turned[:, :, :].rearrange("p k b -> p (k b)")]

        ids_ready = [sem("ids_ready_first"), sem("ids_ready_second")]
        dense_loaded = sem("dense_loaded")
        gathered = [sem(f"gathered_{j}") for j in range(GROUPS)]
        hot_ids_loaded = [sem(f"hot_ids_loaded_{h}") for h in range(HOT)]
        hot_loaded = [sem(f"hot_loaded_{h}") for h in range(HOT)]
        row_no_made = sem("row_no_made")
        row_no_ready = sem("row_no_ready")
        hi_ready = sem("hi_ready")
        lo_ready = sem("lo_ready")
        onehot_ready = sem("onehot_ready")
        onehot_used = sem("onehot_used")
        hotT_ready = sem("hotT_ready")
        tile_hot = sem("tile_hot")
        ident_zero = sem("ident_zero")
        ident_ready = sem("ident_ready")
        w_zeroed = sem("w_zeroed")
        wd_loaded = sem("wd_loaded")
        wdots_loaded = sem("wdots_loaded")
        wmid_loaded = sem("wmid_loaded")
        small_loaded = sem("small_loaded")
        wsum_ready = sem("wsum_ready")
        dense_turned = sem("dense_turned")
        denseT_ready = sem("denseT_ready")
        tile_dense = sem("tile_dense")
        pads_zeroed = sem("pads_zeroed")
        turned_done = sem("turned_done")
        feat_vec = sem("feat_vec")
        feat_act = sem("feat_act")
        gram_done = sem("gram_done")
        dots_vec = sem("dots_vec")
        dots_act = sem("dots_act")
        l1_done = sem("l1_done")
        h1_ready = sem("h1_ready")
        h1_turned_done = sem("h1_turned_done")
        h1T_ready = sem("h1T_ready")
        l2_done = sem("l2_done")
        h2_ready = sem("h2_ready")
        y_ready = sem("y_ready")
        y_stored = sem("y_stored")
        out_written = sem("out_written")

        ids_tiled = ids.rearrange("(p t) f -> p t f", t=TILES)
        ids_src = [ids_tiled[:, :, 0:SPLIT], ids_tiled[:, :, SPLIT:TABLES]]
        half_groups = [range(0, FIRST_HALF), range(FIRST_HALF, GROUPS)]
        EVENS, ODDS = (GROUPS + 1) // 2, GROUPS // 2

        featT_by_feat = featT[:, :, :].rearrange("d b n -> d n b")
        dots_cols = dots[:, :, :].rearrange("p k (c a b s) -> p s c k a b", s=QUAD, c=CHUNKS, a=CHUNK_BANKS)

        def spread(copy, s, c):
            src = gram[c % 2][SLOT * s:SLOT * (s + 1), :, 0:PER_BANK * QUAD * FEATS].rearrange(
                "n a (b e m) -> n e m a b", b=PER_BANK, e=QUAD)
            for r in range(QUAD):
                ks = len(range(r, STARS, QUAD))
                last = copy(dots_cols[SLOT * r:SLOT * (r + 1), s, c, 0:ks],
                            src[:, s, r:r + QUAD * (ks - 1) + 1:QUAD])
            return last

        block = ctx.enter_context(nc.Block())

        @block.sync
        def _(sp):
            def load_hot(i):
                table = tables[HOT_FIRST + i].rearrange("(p c) d -> p c d", c=ROW_BLOCKS)
                sp.dma_start(hot_ids_all[:, i, :], hot_ids[i:i + 1, :].broadcast_to([HOT_P, BATCH])).then_inc(
                    hot_ids_loaded[i], 16)
                for part in (slice(0, HOT_CUT), slice(HOT_CUT, HOT_P)):
                    sp.dma_start(hot_rows[part, i, :, :], table[part]).then_inc(hot_loaded[i], 16)

            sp.dma_start(ids_half[0][:, :], ids_src[0][:, 0, :]).then_inc(ids_ready[0], 16)
            load_hot(0)
            sp.dma_start(ids_half[1][:, :], ids_src[1][:, 0, :]).then_inc(ids_ready[1], 16)
            sp.dma_start(dense_rows[:, :, :], dense.rearrange("(p t) d -> p t d", t=TILES)).then_inc(dense_loaded, 16)
            for i in range(1, HOT):
                load_hot(i)
            sp.dma_start(w_dense[:, 0, :], w1[0:D, :]).then_inc(wd_loaded, 16)
            sp.dma_start(w_dense[:, 1, :], w1[w1.shape[0] - D:, :]).then_inc(wd_loaded, 16)
            sp.wait_ge(w_zeroed, 1)
            row = D
            for m in range(STARS):
                k, r, n = m // QUAD, m % QUAD, FEATS - 1 - m
                sp.dma_start(w_dots[SLOT * r + m + 1:SLOT * r + FEATS, k, :], w1[row:row + n, :]).then_inc(
                    wdots_loaded, 16)
                row += n
            sp.dma_start(b1_col[:, :], b1.rearrange("(c p o) -> p c o", p=P, o=1),
                         allow_slow_non_contiguous=True).then_inc(small_loaded, 16)
            sp.dma_start(b2_all[:, :], b2.rearrange("(o n) -> o n", o=1).broadcast_to([P, H2])).then_inc(small_loaded, 16)
            sp.dma_start(w3_all[:, :], w3.rearrange("n o -> o n").broadcast_to([P, H2])).then_inc(small_loaded, 16)
            sp.dma_start(w_mid[:, :, :], w2.rearrange("(c p) n -> p c n", p=P)).then_inc(wmid_loaded, 16)
            with sp.Fori(1, TILES) as t:
                for h in range(2):
                    sp.wait_ge(w_zeroed, 1)
                    for j in half_groups[h]:
                        sp.wait_ge(gathered[j], 16 * len(MEMBERS[j]) * t)
                    sp.dma_start(ids_half[h][:, :], ids_src[h][:, bass.ds(t, 1), :]).then_inc(ids_ready[h], 16)
            sp.wait_ge(y_stored, TILES)
            sp.dma_start(out.rearrange("(p t) o -> p (t o)", t=TILES), y_all[:, :]).then_inc(out_written, 16)
            sp.wait_ge(out_written, 16)

        @block.gpsimd
        def _(pool):
            nc.gpsimd.memset(ident[:, :], 0.0).then_inc(ident_zero, 1)
            pool.wait_ge(ident_zero, 1)
            nc.gpsimd.affine_select(out=ident[:, :], in_=ident[:, :], compare_op=ALU.not_equal, fill=1.0, base=0,
                                    pattern=[[-1, P]], channel_multiplier=1).then_inc(ident_ready, 1)
            nc.gpsimd.iota(row_no_int[:, :], pattern=[[1, ROW_BLOCKS]], base=0,
                           channel_multiplier=ROW_BLOCKS).then_inc(row_no_made, 1)

            def gather(j):
                h = int(j >= FIRST_HALF)
                for f in MEMBERS[j]:
                    col = f - h * SPLIT
                    pool.indirect_dma_start(rows[:, f, :], None, tables[f],
                                            bass.IndirectOffsetOnAxis(ap=ids_half[h][:, col:col + 1], axis=0)
                                            ).then_inc(gathered[j], 16)

            for j in range(GROUPS):
                if j in (0, FIRST_HALF):
                    pool.wait_ge(ids_ready[int(j > 0)], 16)
                gather(j)
            groups_read = pool.alloc_register("groups_read")
            pool.reg_mov(groups_read, 1)
            with pool.Fori(1, TILES) as t:
                for j in range(GROUPS):
                    if j in (0, FIRST_HALF):
                        pool.wait_ge(ids_ready[int(j > 0)], 16 * (t + 1))
                    pool.wait_ge(turned_done, groups_read)
                    pool.reg_add(groups_read, groups_read, 1)
                    gather(j)

        @block.tensor
        def _(pe):
            def hot(i):
                pe.wait_ge(hi_ready, i + 1)
                pe.wait_ge(lo_ready, i + 1)
                if i >= 2:
                    pe.wait_ge(hotT_ready, i - 1)
                for c in range(ROW_BLOCKS):
                    n = ROW_BLOCKS * i + c
                    pe.wait_ge(onehot_ready, n + 1)
                    nc.tensor.matmul(hot_sum[i % 2], hot_hi[i % 2][:, c, :], onehot[n % ONES][:, :], start=c == 0,
                                     stop=False)
                    nc.tensor.matmul(hot_sum[i % 2], hot_lo[i % 2][:, c, :], onehot[n % ONES][:, :], start=False,
                                     stop=c == ROW_BLOCKS - 1).then_inc(onehot_used, 1)

            def turn(t, j):
                pe.wait_ge(gathered[j], 16 * len(MEMBERS[j]) * (t + 1))
                if j % 2 == 0 and not (isinstance(t, int) and j == 0):
                    pe.wait_ge(feat_vec, EVENS * t + j // 2)
                if j % 2 == 1 and not (isinstance(t, int) and j == 1):
                    pe.wait_ge(feat_act, ODDS * t + j // 2)
                for i, f in enumerate(MEMBERS[j]):
                    last = nc.tensor.transpose(turned[j % 2][:, i, :], rows[:, f, :], ident[:, :])
                last.then_inc(turned_done, 1)

            def dot(t, first=False):
                pe.wait_ge(tile_dense, t + 1)
                pe.wait_ge(tile_hot, t + 1)
                pe.wait_ge(feat_vec, EVENS * (t + 1))
                pe.wait_ge(feat_act, ODDS * (t + 1))
                for c in range(CHUNKS):
                    if not (first and c < 2):
                        done = CHUNKS * t + max(c - 1, 0)
                        pe.wait_ge(dots_vec, done)
                        pe.wait_ge(dots_act, done)
                    for a in range(CHUNK_BANKS):
                        for b in range(PER_BANK):
                            at = QUAD * (CHUNK * c + PER_BANK * a + b)
                            cols = QUAD * FEATS
                            last = nc.tensor.matmul(
                                gram[c % 2][:, a, cols * b:cols * (b + 1)].rearrange("p (s n) -> p s n", s=QUAD),
                                featT[:, at:at + QUAD, :], featT[:, at:at + QUAD, 0:FEATS], start=True, stop=True)
                    last.then_inc(gram_done, 1)

            def first_layer_dense(t):
                pe.wait_ge(tile_dense, t + 1)
                nc.tensor.matmul(layer[:, :], denseT_now[:, :], w_dsum[:, :], start=True, stop=False)

            def first_layer_dots(k):
                kp = SLOT * len(range(QUAD * k, min(QUAD * (k + 1), STARS)))
                last = nc.tensor.matmul(layer[:, :], dots[0:kp, k, :], w_dots[0:kp, k, :], start=False,
                                        stop=k == STEPS - 1)
                if k == STEPS - 1:
                    last.then_inc(l1_done, 1)

            def turn_h1(t):
                pe.wait_ge(h1_ready, t + 1)
                for k in range(K2):
                    last = nc.tensor.transpose(h1_turned[:, k, :], h1[:, P * k:P * (k + 1)], ident[:, :])
                last.then_inc(h1_turned_done, 1)

            def second_layer(t):
                pe.wait_ge(h1T_ready, t + 1)
                for k in range(K2):
                    last = nc.tensor.matmul(layer[:, 0:H2], h1T[:, k, :], w_mid[:, k, :], start=k == 0,
                                            stop=k == K2 - 1)
                last.then_inc(l2_done, 1)

            pe.wait_ge(ident_ready, 1)
            hot(0)
            pe.wait_ge(dense_loaded, 16)
            for t in range(TILES):
                last = nc.tensor.transpose(turned[0][:, t, :], dense_rows[:, t, :], ident[:, :])
            last.then_inc(dense_turned, 1)
            pe.wait_ge(denseT_ready, 1)
            for j in range(GROUPS):
                turn(0, j)
                if j + 1 < HOT:
                    hot(j + 1)
            dot(0, first=True)
            pe.wait_ge(wsum_ready, 1)
            pe.wait_ge(wdots_loaded, 16 * STARS)
            pe.wait_ge(wmid_loaded, 16)
            with pe.Fori(1, TILES) as t:
                turn(t, 0)
                first_layer_dense(t - 1)
                turn(t, 1)
                pe.wait_ge(dots_vec, CHUNKS * t)
                pe.wait_ge(dots_act, CHUNKS * t)
                for k in range(STEPS):
                    first_layer_dots(k)
                    if k == 2:
                        turn(t, 2)
                turn(t, 3)
                turn_h1(t - 1)
                for j in range(4, GROUPS):
                    turn(t, j)
                second_layer(t - 1)
                dot(t)
            first_layer_dense(TILES - 1)
            pe.wait_ge(dots_vec, CHUNKS * TILES)
            pe.wait_ge(dots_act, CHUNKS * TILES)
            for k in range(STEPS):
                first_layer_dots(k)
            turn_h1(TILES - 1)
            second_layer(TILES - 1)

        @block.scalar
        def _(act):
            def hot_upper(i):
                act.wait_ge(hot_loaded[i], 32)
                if i >= 2:
                    act.wait_ge(onehot_used, ROW_BLOCKS * (i - 1))
                nc.scalar.copy(hot_hi[i % 2][:, :, :], hot_rows[:, i, :, :]).then_inc(hi_ready, 1)

            def hot_out(i):
                act.wait_ge(onehot_used, ROW_BLOCKS * (i + 1))
                nc.scalar.copy(hotT[:, i, :, :].rearrange("d t b -> d (t b)"), hot_sum[i % 2]).then_inc(hotT_ready, 1)

            def feats(t, j):
                act.wait_ge(turned_done, GROUPS * t + j + 1)
                for i, f, n in runs(MEMBERS[j]):
                    last = nc.scalar.copy(featT_by_feat[:, 1 + f:1 + f + n], turned[1][:, i:i + n, :])
                last.then_inc(feat_act, 1)

            def feats_hot(t):
                nc.scalar.copy(featT_by_feat[:, 1 + HOT_FIRST:1 + HOT_FIRST + HOT],
                               hotT[:, :, bass.ds(t, 1), :].rearrange("d i t b -> d i (t b)")).then_inc(tile_hot, 1)

            def spreads(t):
                for c in range(CHUNKS):
                    act.wait_ge(gram_done, CHUNKS * t + c + 1)
                    spread(nc.scalar.copy, 2, c)
                    spread(nc.scalar.copy, 3, c).then_inc(dots_act, 1)

            def h1_relu(t):
                act.wait_ge(h1_turned_done, t + 1)
                for k in range(K2):
                    last = nc.scalar.activation(h1T[:, k, :], h1_turned[:, k, :], ACT.Relu, bias=b1_col[:, k:k + 1])
                last.then_inc(h1T_ready, 1)

            hot_upper(0)
            for j in range(max(GROUPS, HOT)):
                if j + 1 < HOT:
                    hot_upper(j + 1)
                if j < HOT:
                    hot_out(j)
                if j % 2 == 1 and j < GROUPS:
                    feats(0, j)
            act.wait_ge(hotT_ready, HOT)
            feats_hot(0)
            spreads(0)
            act.wait_ge(small_loaded, 16 * 3)
            with act.Fori(1, TILES) as t:
                act.wait_ge(gram_done, CHUNKS * t)
                feats_hot(t)
                feats(t, 1)
                feats(t, 3)
                h1_relu(t - 1)
                for j in range(5, GROUPS, 2):
                    feats(t, j)
                act.wait_ge(l1_done, t)
                spreads(t)
            h1_relu(TILES - 1)

        @block.vector
        def _(dve):
            def hot_lower(i):
                dve.wait_ge(hi_ready, i + 1)
                if i >= 2:
                    dve.wait_ge(onehot_used, ROW_BLOCKS * (i - 1))
                nc.vector.tensor_sub(hot_lo[i % 2][:, :, :], hot_rows[:, i, :, :],
                                     hot_hi[i % 2][:, :, :].bitcast(FP32)).then_inc(lo_ready, 1)

            def hot_onehots(i, blocks):
                dve.wait_ge(hot_ids_loaded[i], 16)
                for c in blocks:
                    n = ROW_BLOCKS * i + c
                    if n >= ONES:
                        dve.wait_ge(onehot_used, n - ONES + 1)
                    nc.vector.tensor_scalar(onehot[n % ONES][:, :], hot_ids_all[:, i, :], row_no[:, c:c + 1], None,
                                            op0=ALU.is_equal).then_inc(onehot_ready, 1)

            def dense_now(t, out):
                return nc.vector.tensor_copy(out, denseT[:, bass.ds(t, 1), :].rearrange("d t b -> d (t b)"))

            def feats(t, j):
                dve.wait_ge(turned_done, GROUPS * t + j + 1)
                for i, f, n in runs(MEMBERS[j]):
                    last = nc.vector.tensor_copy(featT_by_feat[:, 1 + f:1 + f + n], turned[0][:, i:i + n, :])
                last.then_inc(feat_vec, 1)

            def spreads(t):
                for c in range(CHUNKS):
                    dve.wait_ge(gram_done, CHUNKS * t + c + 1)
                    spread(nc.vector.tensor_copy, 0, c)
                    spread(nc.vector.tensor_copy, 1, c).then_inc(dots_vec, 1)

            def h1_copy(t):
                dve.wait_ge(l1_done, t + 1)
                nc.vector.tensor_copy(h1[:, :], layer[:, :]).then_inc(h1_ready, 1)

            def last_layer(t):
                dve.wait_ge(l2_done, t + 1)
                nc.vector.tensor_add(h2[:, :], layer[:, 0:H2], b2_all[:, :]).then_inc(h2_ready, 1)
                dve.wait_ge(h2_ready, t + 1)
                nc.vector.scalar_tensor_tensor(h2w[:, :], h2[:, :], 0.0, w3_all[:, :], op0=ALU.max, op1=ALU.mult,
                                               accum_out=y_now[:, :]).then_inc(y_ready, 1)
                dve.wait_ge(y_ready, t + 1)
                nc.vector.tensor_copy(y_all[:, bass.ds(t, 1)], y_now[:, :]).then_inc(y_stored, 1)

            nc.vector.memset(w_dots[:, :, :], 0.0).then_inc(w_zeroed, 1)
            nc.vector.memset(featT[:, :, FEATS:SLOT], 0.0).then_inc(pads_zeroed, 1)
            dve.wait_ge(row_no_made, 1)
            nc.vector.tensor_copy(row_no[:, :], row_no_int[:, :]).then_inc(row_no_ready, 1)
            dve.wait_ge(row_no_ready, 1)
            hot_lower(0)
            hot_onehots(0, range(ROW_BLOCKS))
            dve.wait_ge(dense_turned, 1)
            nc.vector.tensor_copy(denseT[:, :, :], turned[0][:, :, :]).then_inc(denseT_ready, 1)
            dve.wait_ge(denseT_ready, 1)
            dense_now(0, denseT_now[:, :])
            dense_now(0, featT[:, :, 0]).then_inc(tile_dense, 1)
            for j in range(max(GROUPS, HOT)):
                if j + 1 < HOT:
                    hot_lower(j + 1)
                    hot_onehots(j + 1, range(0, ONES))
                if j % 2 == 0 and j < GROUPS:
                    feats(0, j)
                if j + 1 < HOT:
                    hot_onehots(j + 1, range(ONES, ROW_BLOCKS))
            dve.wait_ge(wd_loaded, 32)
            nc.vector.tensor_add(w_dsum[:, :], w_dense[:, 0, :], w_dense[:, 1, :]).then_inc(wsum_ready, 1)
            dve.wait_ge(small_loaded, 16 * 3)
            spreads(0)
            with dve.Fori(1, TILES) as t:
                dve.wait_ge(gram_done, CHUNKS * t)
                feats(t, 0)
                feats(t, 2)
                h1_copy(t - 1)
                dense_now(t, denseT_now[:, :])
                dense_now(t, featT[:, :, 0]).then_inc(tile_dense, 1)
                for j in range(4, GROUPS, 2):
                    feats(t, j)
                last_layer(t - 1)
                spreads(t)
            h1_copy(TILES - 1)
            last_layer(TILES - 1)


def kernel(**inputs):
    import concourse.bacc as bacc
    from concourse.bass_utils import run_bass_kernel_spmd

    nc = bacc.Bacc("TRN2", target_bir_lowering=False, num_devices=1)
    arrays = {}

    def given(name):
        a = np.ascontiguousarray(inputs[name])
        arrays[f"in_{name}"] = a
        return nc.dram_tensor(f"in_{name}", a.shape, mybir.dt.from_np(a.dtype), kind="ExternalInput").ap()

    ids = given("ids")
    hot = np.asarray(inputs["ids"])[:, HOT_FIRST:HOT_FIRST + HOT].reshape(P, TILES, HOT).transpose(2, 1, 0)
    arrays["in_hot_ids"] = np.ascontiguousarray(hot).reshape(HOT, BATCH)
    hot_ids = nc.dram_tensor("in_hot_ids", (HOT, BATCH), mybir.dt.from_np(arrays["in_hot_ids"].dtype),
                             kind="ExternalInput").ap()
    tables = [given(f"tbl_{f}") for f in range(TABLES)]
    dense, w1, b1, w2, b2, w3 = (given(n) for n in ("r_dense_features", "W_top1", "b_top1", "W_top2", "b_top2",
                                                    "W_top3"))
    out = nc.dram_tensor("out", (BATCH, 1), FP32, kind="ExternalOutput").ap()
    build(nc, ids, hot_ids, tables, dense, w1, b1, w2, b2, w3, out)
    return run_bass_kernel_spmd(nc, [arrays], core_ids=[0]).results[0]["out"]
```

```python
import numpy as np
import concourse.bass as bass
from concourse import mybir
from contextlib import ExitStack

FP32 = mybir.dt.float32
FP32R = mybir.dt.float32r
INT32 = mybir.dt.int32
ALU = mybir.AluOpType
ACT = mybir.ActivationFunctionType

P = 128
D = 128
TABLES = 26
FEATS = TABLES + 1
SLOT = 32
BATCH = 512
TILES = BATCH // P
H1, H2 = 512, 256
K2 = H1 // P

HOT_TABLES = [5, 10, 20, 21, 22, 23, 24]
HOT_ROWS = [1000, 1000, 1250, 1250, 1250, 1250, 1250]
HOT = len(HOT_TABLES)
HOT_P = 125
BLOCKS = [n // HOT_P for n in HOT_ROWS]
LAYOUTS = sorted(set(BLOCKS))
MAX_BLOCKS = max(BLOCKS)
HOT_CUT = 112
ROW_BUFFERS = 5
ONES = 6
AHEAD = 4
ACT_BLOCKS = 2
VEC_BLOCKS = [n - ACT_BLOCKS for n in BLOCKS]
HALVES = [(0, BLOCKS[0] // 2), (BLOCKS[0] // 2, BLOCKS[0])]
WARM_UP = 36

GATHERED = [f for f in range(TABLES) if f not in HOT_TABLES]
GROUP = 4
MEMBERS = [GATHERED[i:i + GROUP] for i in range(0, len(GATHERED), GROUP)]
GROUPS = len(MEMBERS)
FIRST_HALF = GROUPS // 2
SPLIT = MEMBERS[FIRST_HALF][0]
W_FIRST = 4
NEXT_IDS_AFTER = [3, 5]

QUAD = P // SLOT
GRAMS = P // QUAD
PER_BANK = 4
CHUNK_BANKS = 2
CHUNK = PER_BANK * CHUNK_BANKS
CHUNKS = GRAMS // CHUNK

STARS = 20
STEPS = STARS // QUAD
REPEATED = range(STARS + 1, FEATS - 1)
LONE_PAIR = (STARS, FEATS - 1)
TURN_BEFORE = [0, 2, 3]


def pair_row(m, n):
    return D + sum(FEATS - 1 - i for i in range(m)) + n - m - 1


def runs(members):
    out = []
    for i, f in enumerate(members):
        if out and f == out[-1][1] + out[-1][2]:
            out[-1][2] += 1
        else:
            out.append([i, f, 1])
    return out


def build(nc, ids, hot_ids, tables, dense, w1, b1, w2, b2, w3, out):
    ctx = ExitStack()
    with ctx:
        def sb(name, shape, dt=FP32):
            return ctx.enter_context(nc.sbuf_tensor(name, shape, dt))

        def ps(name, shape):
            return ctx.enter_context(nc.psum_tensor(name, shape, FP32))

        def sem(name):
            return ctx.enter_context(nc.semaphore(name))

        ids_half = [sb("ids_first", [P, SPLIT], INT32), sb("ids_second", [P, TABLES - SPLIT], INT32)]
        rows = sb("rows", [P, TABLES, D])
        dense_rows = sb("dense_rows", [P, TILES, D])
        hot_ids_all = sb("hot_ids_all", [HOT_P, HOT, BATCH], INT32)
        hot_rows = sb("hot_rows", [HOT_P, ROW_BUFFERS, MAX_BLOCKS, D])
        hot_hi = [sb(f"hot_hi_{i}", [HOT_P, MAX_BLOCKS, D], FP32R) for i in range(2)]
        hot_lo = [sb(f"hot_lo_{i}", [HOT_P, MAX_BLOCKS, D], FP32R) for i in range(2)]
        onehot = [sb(f"onehot_{i}", [HOT_P, BATCH], FP32R) for i in range(ONES)]
        onehot_act = [sb(f"onehot_act_{i}", [HOT_P, BATCH], FP32R) for i in range(2 * ACT_BLOCKS)]
        distance = sb("distance", [HOT_P, ACT_BLOCKS, BATCH])
        row_no_int = sb("row_no_int", [HOT_P, len(LAYOUTS), MAX_BLOCKS], INT32)
        row_no_neg = sb("row_no_neg", [HOT_P, len(LAYOUTS), MAX_BLOCKS])
        row_no = sb("row_no", [HOT_P, len(LAYOUTS), MAX_BLOCKS])
        hotT = sb("hotT", [D, HOT, TILES, P])
        ident = sb("ident", [P, P])
        denseT = sb("denseT", [D, TILES, P])
        dense_hi = sb("dense_hi", [D, P], FP32R)
        dense_lo = sb("dense_lo", [D, P], FP32R)
        featT = sb("featT", [D, P, SLOT])
        dots = sb("dots", [P, STEPS, P])
        dots_hi = sb("dots_hi", [P, STEPS, P], FP32R)
        dots_lo = sb("dots_lo", [P, STEPS, P], FP32R)
        w_dense = sb("w_dense", [P, 2, H1])
        w_dsum = sb("w_dsum", [P, H1])
        w_dots = sb("w_dots", [P, STEPS, H1])
        w_dsum_hi = sb("w_dsum_hi", [P, H1], FP32R)
        w_dsum_lo = sb("w_dsum_lo", [P, H1], FP32R)
        w_dots_hi = sb("w_dots_hi", [P, STEPS, H1], FP32R)
        w_dots_lo = sb("w_dots_lo", [P, STEPS, H1], FP32R)
        w_lone = sb("w_lone", [P, H1])
        lone_product = sb("lone_product", [P, D])
        lone_dot = sb("lone_dot", [P, 1])
        w_mid = sb("w_mid", [P, K2, H2])
        b1_col = sb("b1_col", [P, K2])
        b2_all = sb("b2_all", [P, H2])
        w3_all = sb("w3_all", [P, H2])
        h1 = sb("h1", [P, H1])
        h1T = sb("h1T", [P, K2, P])
        h2 = sb("h2", [P, H2])
        h2w = sb("h2w", [P, H2])
        ones_row = sb("ones_row", [1, P])
        y_now = sb("y_now", [P, 1])
        y_all = sb("y_all", [P, TILES])

        turned = [ps("turned_even", [P, GROUP, P]), ps("turned_odd", [P, GROUP, P])]
        gram = [ps("gram_even", [P, CHUNK_BANKS, P * PER_BANK]), ps("gram_odd", [P, CHUNK_BANKS, P * PER_BANK])]
        layer = ps("layer", [P, H1])
        h1_turned = ps("h1_turned", [P, K2, P])
        hot_sum = [layer[:, :], h1_turned[:, :, :].rearrange("p k b -> p (k b)")]
        layer2 = h1_turned[:, 0:H2 // P, :].rearrange("p k b -> p (k b)")
        last_halves = [layer[:, 0:H1 // 2], gram[0][:, 1, 0:H1 // 2]]
        last_turned = [h1_turned[:, 0, :], turned[0][:, 0, :], turned[1][:, 0, :], gram[0][:, 0, 0:P]]
        last_layer2 = gram[1][:, 0, 0:H2]

        ids_ready = [sem("ids_ready_first"), sem("ids_ready_second")]
        dense_loaded = sem("dense_loaded")
        gathered = [sem(f"gathered_{j}") for j in range(GROUPS)]
        hot_ids_loaded = [sem(f"hot_ids_loaded_{h}") for h in range(HOT)]
        hot_loaded = [sem(f"hot_loaded_{h}") for h in range(HOT)]
        row_no_made = sem("row_no_made")
        row_no_ready = sem("row_no_ready")
        hi_ready = sem("hi_ready")
        lo_ready = sem("lo_ready")
        onehot_ready = sem("onehot_ready")
        distance_ready = sem("distance_ready")
        onehot_act_ready = sem("onehot_act_ready")
        onehot_used = sem("onehot_used")
        hot_half_loaded = sem("hot_half_loaded")
        hotT_ready = sem("hotT_ready")
        tile_hot = sem("tile_hot")
        ident_zero = sem("ident_zero")
        ident_ready = sem("ident_ready")
        w_zeroed = sem("w_zeroed")
        wd_loaded = sem("wd_loaded")
        wdots_loaded = sem("wdots_loaded")
        wmid_loaded = sem("wmid_loaded")
        small_loaded = sem("small_loaded")
        wsum_ready = sem("wsum_ready")
        w_hi_ready = sem("w_hi_ready")
        w_lo_ready = sem("w_lo_ready")
        dense_turned = sem("dense_turned")
        denseT_ready = sem("denseT_ready")
        tile_dense = sem("tile_dense")
        dense_hi_ready = sem("dense_hi_ready")
        dense_parts_ready = sem("dense_parts_ready")
        dots_zeroed = sem("dots_zeroed")
        ones_made = sem("ones_made")
        turned_done = sem("turned_done")
        feat_vec = sem("feat_vec")
        feat_act = sem("feat_act")
        gram_done = sem("gram_done")
        spare_vec = sem("spare_vec")
        spare_act = sem("spare_act")
        dots_vec = sem("dots_vec")
        dots_act = sem("dots_act")
        lone_ready = sem("lone_ready")
        dots_hi_ready = sem("dots_hi_ready")
        dots_lo_ready = sem("dots_lo_ready")
        l1_done = sem("l1_done")
        h1_ready = sem("h1_ready")
        h1_turned_done = sem("h1_turned_done")
        h1T_ready = sem("h1T_ready")
        last_half_done = sem("last_half_done")
        last_half_ready = sem("last_half_ready")
        last_turned_act = sem("last_turned_act")
        last_turned_vec = sem("last_turned_vec")
        last_h1T_act = sem("last_h1T_act")
        last_h1T_vec = sem("last_h1T_vec")
        last_sum_done = sem("last_sum_done")
        l2_done = sem("l2_done")
        h2_ready = sem("h2_ready")
        y_ready = sem("y_ready")
        y_stored = sem("y_stored")
        out_written = sem("out_written")

        ids_tiled = ids.rearrange("(p t) f -> p t f", t=TILES)
        ids_src = [ids_tiled[:, :, 0:SPLIT], ids_tiled[:, :, SPLIT:TABLES]]
        half_groups = [range(0, FIRST_HALF), range(FIRST_HALF, GROUPS)]
        EVENS, ODDS = (GROUPS + 1) // 2, GROUPS // 2

        featT_by_feat = featT[:, :, :].rearrange("d b n -> d n b")
        dots_cols = dots[:, :, :].rearrange("p k (c a b s) -> p s c k a b", s=QUAD, c=CHUNKS, a=CHUNK_BANKS)

        def spread(engine, copy, quadrants, t, c, spare_copied):
            def quadrant(s):
                return gram[c % 2][SLOT * s:SLOT * (s + 1), :, 0:PER_BANK * QUAD * FEATS].rearrange(
                    "n a (b e m) -> n e m a b", b=PER_BANK, e=QUAD)[:, s]

            for s in quadrants:
                for r in range(QUAD):
                    n = len(range(STARS + r, FEATS, QUAD))
                    last = copy(dots_cols[SLOT * r:SLOT * (r + 1), s, c, 0:n], quadrant(s)[:, STARS + r:FEATS:QUAD])
                last.then_inc(spare_copied, 1)
            for i, s in enumerate(quadrants):
                engine.wait_ge(spare_copied, len(quadrants) * (CHUNKS * t + c) + i + 1)
                for r in range(QUAD):
                    last = copy(dots_cols[SLOT * r:SLOT * r + FEATS, s, c], quadrant(s)[0:FEATS, r:STARS:QUAD])
            return last

        dense_turned_at = gram[0][:, 0, :].rearrange("p (t b) -> p t b", t=TILES)

        def first_tile_groups(i):
            return range(i - 1, i if i < HOT - 1 else GROUPS)

        def parts_of(i, c):
            return 1 if (i, c) < (0, HALVES[1][0]) else i + 2

        def blocks_to(i, c=0):
            return sum(BLOCKS[:i]) + c

        def vec_to(i, c=0):
            return sum(VEC_BLOCKS[:i]) + c

        block = ctx.enter_context(nc.Block())

        @block.sync
        def _(sp):
            def load_hot(i):
                table = tables[HOT_TABLES[i]].rearrange("(p c) d -> p c d", c=BLOCKS[i])
                sp.dma_start(hot_ids_all[:, i, :], hot_ids[i:i + 1, :].broadcast_to([HOT_P, BATCH])).then_inc(
                    hot_ids_loaded[i], 16)
                for n, (a, b) in enumerate(HALVES if i == 0 else [(0, BLOCKS[i])]):
                    for part in (slice(0, HOT_CUT), slice(HOT_CUT, HOT_P)):
                        sp.dma_start(hot_rows[part, i % ROW_BUFFERS, a:b, :], table[part, a:b, :]).then_inc(
                            hot_half_loaded if (i, n) == (0, 0) else hot_loaded[i], 16)

            sp.dma_start(ids_half[0][:, :], ids_src[0][:, 0, :]).then_inc(ids_ready[0], 16)
            load_hot(0)
            sp.dma_start(ids_half[1][:, :], ids_src[1][:, 0, :]).then_inc(ids_ready[1], 16)
            load_hot(1)
            sp.dma_start(dense_rows[:, :, :], dense.rearrange("(p t) d -> p t d", t=TILES)).then_inc(dense_loaded, 16)
            load_hot(2)
            sp.dma_start(w_dense[:, 0, :], w1[0:D, :]).then_inc(wd_loaded, 16)
            sp.dma_start(w_dense[:, 1, :], w1[w1.shape[0] - D:, :]).then_inc(wd_loaded, 16)
            sp.wait_ge(w_zeroed, 1)
            m = 0
            for i in range(2, HOT):
                if i > 2:
                    sp.wait_ge(onehot_used, blocks_to(i - 3, 1))
                    load_hot(i)
                while m < STARS * (i - 1) // (HOT - 2):
                    k, r, n = m // QUAD, m % QUAD, FEATS - 1 - m
                    sp.dma_start(w_dots[SLOT * r + m + 1:SLOT * r + FEATS, k, :], w1[pair_row(m, m + 1):pair_row(m, m + 1) + n, :]
                                 ).then_inc(wdots_loaded, 16)
                    m += 1
                if i in NEXT_IDS_AFTER:
                    h = NEXT_IDS_AFTER.index(i)
                    for j in half_groups[h]:
                        sp.wait_ge(gathered[j], 16 * len(MEMBERS[j]))
                    sp.dma_start(ids_half[h][:, :], ids_src[h][:, 1, :]).then_inc(ids_ready[h], 16)
            for m in range(STARS, FEATS - 2):
                first = max(m + 1, REPEATED.start)
                k, r, n = (m - STARS) // QUAD, m % QUAD, REPEATED.stop - first
                sp.dma_start(w_dots[SLOT * (r + 1) - n:SLOT * (r + 1), k, :],
                             w1[pair_row(m, first):pair_row(m, first) + n, :]).then_inc(wdots_loaded, 16)
            last = FEATS - 1
            for m in REPEATED:
                k, at = (last - STARS) // QUAD, SLOT * (last % QUAD) + FEATS + m - REPEATED.start
                sp.dma_start(w_dots[at:at + 1, k, :], w1[pair_row(m, last):pair_row(m, last) + 1, :]).then_inc(
                    wdots_loaded, 16)
            lone = pair_row(*LONE_PAIR)
            sp.dma_start(w_lone[:, :], w1[lone:lone + 1, :].broadcast_to([P, H1])).then_inc(small_loaded, 16)
            sp.dma_start(b1_col[:, :], b1.rearrange("(c p o) -> p c o", p=P, o=1),
                         allow_slow_non_contiguous=True).then_inc(small_loaded, 16)
            sp.dma_start(b2_all[:, :], b2.rearrange("(o n) -> o n", o=1).broadcast_to([P, H2])).then_inc(small_loaded, 16)
            sp.dma_start(w3_all[:, :], w3.rearrange("n o -> o n").broadcast_to([P, H2])).then_inc(small_loaded, 16)
            sp.dma_start(w_mid[:, :, :], w2.rearrange("(c p) n -> p c n", p=P)).then_inc(wmid_loaded, 16)
            with sp.Fori(2, TILES) as t:
                for h in range(2):
                    sp.wait_ge(w_zeroed, 1)
                    for j in half_groups[h]:
                        sp.wait_ge(gathered[j], 16 * len(MEMBERS[j]) * t)
                    sp.dma_start(ids_half[h][:, :], ids_src[h][:, bass.ds(t, 1), :]).then_inc(ids_ready[h], 16)
            sp.wait_ge(y_stored, TILES)
            sp.dma_start(out.rearrange("(p t) o -> p (t o)", t=TILES), y_all[:, :]).then_inc(out_written, 16)
            sp.wait_ge(out_written, 16)

        @block.gpsimd
        def _(pool):
            nc.gpsimd.memset(ident[:, :], 0.0).then_inc(ident_zero, 1)
            pool.wait_ge(ident_zero, 1)
            nc.gpsimd.affine_select(out=ident[:, :], in_=ident[:, :], compare_op=ALU.not_equal, fill=1.0, base=0,
                                    pattern=[[-1, P]], channel_multiplier=1).then_inc(ident_ready, 1)
            for n, blocks in enumerate(LAYOUTS):
                nc.gpsimd.iota(row_no_int[:, n, :], pattern=[[1, MAX_BLOCKS]], base=0,
                               channel_multiplier=blocks).then_inc(row_no_made, 1)

            def gather(j):
                h = int(j >= FIRST_HALF)
                for f in MEMBERS[j]:
                    col = f - h * SPLIT
                    pool.indirect_dma_start(rows[:, f, :], None, tables[f],
                                            bass.IndirectOffsetOnAxis(ap=ids_half[h][:, col:col + 1], axis=0)
                                            ).then_inc(gathered[j], 16)

            for j in range(GROUPS):
                if j in (0, FIRST_HALF):
                    pool.wait_ge(ids_ready[int(j > 0)], 16)
                gather(j)
            groups_read = pool.alloc_register("groups_read")
            lone_read = pool.alloc_register("lone_read")
            pool.reg_mov(groups_read, 1)
            pool.reg_mov(lone_read, 1)
            with pool.Fori(1, TILES) as t:
                for j in range(GROUPS):
                    if j in (0, FIRST_HALF):
                        pool.wait_ge(ids_ready[int(j > 0)], 16 * (t + 1))
                    pool.wait_ge(turned_done, groups_read)
                    pool.reg_add(groups_read, groups_read, 1)
                    if j == GROUPS - 1:
                        pool.wait_ge(lone_ready, lone_read)
                        pool.reg_add(lone_read, lone_read, 1)
                    gather(j)

        @block.tensor
        def _(pe):
            def hot(i):
                if i >= 2:
                    pe.wait_ge(hotT_ready, i - 1)
                for c in range(BLOCKS[i]):
                    if c == 0 or (i, c) == (0, HALVES[1][0]):
                        pe.wait_ge(hi_ready, parts_of(i, c))
                        pe.wait_ge(lo_ready, parts_of(i, c))
                    if c < VEC_BLOCKS[i]:
                        n = vec_to(i, c)
                        ones = onehot[n % ONES]
                        pe.wait_ge(onehot_ready, n + 1)
                    else:
                        n = ACT_BLOCKS * i + c - VEC_BLOCKS[i]
                        ones = onehot_act[n % len(onehot_act)]
                        pe.wait_ge(onehot_act_ready, n + 1)
                    nc.tensor.matmul(hot_sum[i % 2], hot_hi[i % 2][:, c, :], ones[:, :], start=c == 0, stop=False)
                    nc.tensor.matmul(hot_sum[i % 2], hot_lo[i % 2][:, c, :], ones[:, :], start=False,
                                     stop=c == BLOCKS[i] - 1).then_inc(onehot_used, 1)

            def turn(t, j):
                pe.wait_ge(gathered[j], 16 * len(MEMBERS[j]) * (t + 1))
                first = isinstance(t, int) and t == 0
                if j % 2 == 0 and not (first and j == 0):
                    pe.wait_ge(feat_vec, EVENS * t + j // 2)
                if j % 2 == 1 and not (first and j == 1):
                    pe.wait_ge(feat_act, ODDS * t + j // 2)
                for i, f in enumerate(MEMBERS[j]):
                    last = nc.tensor.transpose(turned[j % 2][:, i, :], rows[:, f, :], ident[:, :])
                last.then_inc(turned_done, 1)

            def dot(t, first=False, more=True):
                pe.wait_ge(tile_dense, t + 1)
                pe.wait_ge(tile_hot, t + 1)
                pe.wait_ge(feat_vec, EVENS * (t + 1))
                pe.wait_ge(feat_act, ODDS * (t + 1))
                for c in range(CHUNKS):
                    if not (first and c < 2):
                        done = CHUNKS * t + max(c - 1, 0)
                        pe.wait_ge(dots_vec, done)
                        pe.wait_ge(dots_act, done)
                    for a in range(CHUNK_BANKS):
                        for b in range(PER_BANK):
                            at = QUAD * (CHUNK * c + PER_BANK * a + b)
                            cols = QUAD * FEATS
                            last = nc.tensor.matmul(
                                gram[c % 2][:, a, cols * b:cols * (b + 1)].rearrange("p (s n) -> p s n", s=QUAD),
                                featT[:, at:at + QUAD, :], featT[:, at:at + QUAD, 0:FEATS], start=True, stop=True)
                    last.then_inc(gram_done, 1)
                    if c == 1 and not first:
                        turn_h1(t - 1)
                    if c >= CHUNKS - 2 and more:
                        turn(t + 1, c - (CHUNKS - 2))

            def three_passes(out, x_hi, x_lo, w_hi, w_lo, lo_ready=None, start=False, stop=False):
                nc.tensor.matmul(out, x_hi, w_hi, start=start, stop=False)
                nc.tensor.matmul(out, x_hi, w_lo, start=False, stop=False)
                if lo_ready is not None:
                    pe.wait_ge(dots_lo_ready, lo_ready)
                return nc.tensor.matmul(out, x_lo, w_hi, start=False, stop=stop)

            def first_layer_dense(t, out=layer[:, :], cols=slice(0, H1)):
                pe.wait_ge(dense_parts_ready, t + 1)
                three_passes(out, dense_hi[:, :], dense_lo[:, :], w_dsum_hi[:, cols], w_dsum_lo[:, cols], start=True)

            def first_layer_dots(t, k, out=layer[:, :], cols=slice(0, H1)):
                pe.wait_ge(dots_hi_ready, STEPS * t + k + 1)
                return three_passes(out, dots_hi[:, k, :], dots_lo[:, k, :], w_dots_hi[:, k, cols],
                                    w_dots_lo[:, k, cols], lo_ready=STEPS * t + k + 1, stop=k == STEPS - 1)

            def turn_h1(t):
                pe.wait_ge(h1_ready, t + 1)
                for k in range(K2):
                    last = nc.tensor.transpose(h1_turned[:, k, :], h1[:, P * k:P * (k + 1)], ident[:, :])
                last.then_inc(h1_turned_done, 1)

            def second_layer(t):
                pe.wait_ge(h1T_ready, t + 1)
                for k in range(K2):
                    last = nc.tensor.matmul(layer2, h1T[:, k, :], w_mid[:, k, :], start=k == 0, stop=k == K2 - 1)
                last.then_inc(l2_done, 1)

            def last_dense_layers():
                t, half = TILES - 1, H1 // 2
                for h, out in enumerate(last_halves):
                    if h == 1:
                        pe.wait_ge(dots_vec, CHUNKS * TILES - 1)
                        pe.wait_ge(dots_act, CHUNKS * TILES - 1)
                    first_layer_dense(t, out, slice(half * h, half * (h + 1)))
                for k in range(STEPS):
                    for h, out in enumerate(last_halves):
                        last = first_layer_dots(t, k, out, slice(half * h, half * (h + 1)))
                        if k == STEPS - 1:
                            last.then_inc(last_half_done, 1)
                nc.tensor.matmul(last_layer2, ones_row[:, :], b2_all[0:1, :], start=True, stop=False)
                for k in range(K2):
                    if k % (K2 // 2) == 0:
                        pe.wait_ge(last_half_ready, 1 + k // (K2 // 2))
                    nc.tensor.transpose(last_turned[k], h1[:, P * k:P * (k + 1)], ident[:, :]).then_inc(
                        (last_turned_act, last_turned_vec)[k % 2], 1)
                for k in range(K2):
                    pe.wait_ge((last_h1T_act, last_h1T_vec)[k % 2], 1 + k // 2)
                    last = nc.tensor.matmul(last_layer2, h1T[:, k, :], w_mid[:, k, :], start=False, stop=k == K2 - 1)
                last.then_inc(last_sum_done, 1)

            def tile(t, more):
                first_layer_dense(t - 1)
                for k in range(STEPS):
                    if k in TURN_BEFORE:
                        turn(t, 2 + TURN_BEFORE.index(k))
                    last = first_layer_dots(t - 1, k)
                last.then_inc(l1_done, 1)
                dot(t, more=more)
                second_layer(t - 1)

            pe.wait_ge(ident_ready, 1)
            for _ in range(WARM_UP):
                nc.tensor.transpose(turned[0][:, 0, :], ident[:, :], ident[:, :])
            hot(0)
            pe.wait_ge(dense_loaded, 16)
            for t in range(TILES):
                last = nc.tensor.transpose(dense_turned_at[:, t, :], dense_rows[:, t, :], ident[:, :])
            last.then_inc(dense_turned, 1)
            for i in range(1, HOT):
                for j in first_tile_groups(i):
                    turn(0, j)
                hot(i)
            turn(1, 0)
            turn(1, 1)
            dot(0, first=True, more=False)
            pe.wait_ge(hotT_ready, HOT)
            pe.wait_ge(w_lo_ready, 1 + STEPS)
            pe.wait_ge(wmid_loaded, 16)
            pe.wait_ge(ones_made, 1)
            pe.wait_ge(small_loaded, 16 * 4)
            with pe.Fori(1, TILES - 1) as t:
                tile(t, more=True)
            tile(TILES - 1, more=False)
            last_dense_layers()

        @block.scalar
        def _(act):
            def hot_upper(i):
                if i >= 2:
                    act.wait_ge(onehot_used, blocks_to(i - 1))
                for a, b in HALVES if i == 0 else [(0, BLOCKS[i])]:
                    act.wait_ge(hot_half_loaded if (i, a) == (0, 0) else hot_loaded[i], 32)
                    nc.scalar.copy(hot_hi[i % 2][:, a:b, :], hot_rows[:, i % ROW_BUFFERS, a:b, :]).then_inc(hi_ready, 1)

            def hot_onehots(i):
                act.wait_ge(hot_ids_loaded[i], 16)
                if i >= 1:
                    act.wait_ge(onehot_act_ready, ACT_BLOCKS * i)
                for b in range(ACT_BLOCKS):
                    nc.scalar.activation(distance[:, b, :], hot_ids_all[:, i, :], ACT.Abs,
                                         bias=row_no_neg[:, LAYOUTS.index(BLOCKS[i]), VEC_BLOCKS[i] + b:VEC_BLOCKS[i] + b + 1]
                                         ).then_inc(distance_ready, 1)
                if i >= 2:
                    act.wait_ge(onehot_used, blocks_to(i - 1))
                for b in range(ACT_BLOCKS):
                    n = ACT_BLOCKS * i + b
                    act.wait_ge(distance_ready, n + 1)
                    nc.scalar.activation(onehot_act[n % len(onehot_act)][:, :], distance[:, b, :], ACT.Relu,
                                         bias=1.0, scale=-1.0).then_inc(onehot_act_ready, 1)

            def hot_out(i):
                act.wait_ge(onehot_used, blocks_to(i + 1))
                nc.scalar.copy(hotT[:, i, :, :].rearrange("d t b -> d (t b)"), hot_sum[i % 2]).then_inc(hotT_ready, 1)

            def feats(t, j):
                act.wait_ge(turned_done, GROUPS * t + j + 1)
                for i, f, n in runs(MEMBERS[j]):
                    last = nc.scalar.copy(featT_by_feat[:, 1 + f:1 + f + n], turned[1][:, i:i + n, :])
                last.then_inc(feat_act, 1)

            def feats_hot(src, hot):
                for i, f, n in runs([HOT_TABLES[i] for i in hot]):
                    last = nc.scalar.copy(featT_by_feat[:, 1 + f:1 + f + n], src[:, i:i + n])
                again = [f for f in REPEATED if HOT_TABLES.index(f - 1) in hot]
                slot, at = FEATS + again[0] - REPEATED.start, HOT_TABLES.index(again[0] - 1) - hot[0]
                last = nc.scalar.copy(featT_by_feat[:, slot:slot + len(again)], src[:, at:at + len(again)])
                return last

            def hot_tile(t):
                src = hotT[:, :, bass.ds(t, 1), :].rearrange("d i t b -> d i (t b)")
                feats_hot(src, range(HOT)).then_inc(tile_hot, 1)

            def spread_chunk(t, c):
                act.wait_ge(gram_done, CHUNKS * t + c + 1)
                spread(act, nc.scalar.copy, (2, 3), t, c, spare_act).then_inc(dots_act, 1)

            def dots_upper(t):
                act.wait_ge(dots_act, CHUNKS * (t + 1))
                act.wait_ge(dots_vec, CHUNKS * (t + 1))
                for k in range(STEPS):
                    nc.scalar.copy(dots_hi[:, k, :], dots[:, k, :]).then_inc(dots_hi_ready, 1)

            def h1_relu(t):
                act.wait_ge(h1_turned_done, t + 1)
                for k in range(K2):
                    last = nc.scalar.activation(h1T[:, k, :], h1_turned[:, k, :], ACT.Relu, bias=b1_col[:, k:k + 1])
                last.then_inc(h1T_ready, 1)

            hot_upper(0)
            act.wait_ge(row_no_ready, 2)
            hot_onehots(0)
            for i in range(1, HOT):
                hot_upper(i)
                hot_onehots(i)
                hot_out(i - 1)
                for j in first_tile_groups(i):
                    if j % 2 == 1:
                        feats(0, j)
                if i == 1:
                    act.wait_ge(dense_turned, 1)
                    nc.scalar.copy(denseT[:, :, :], dense_turned_at).then_inc(denseT_ready, 1)
            act.wait_ge(wdots_loaded, 16 * (FEATS - 2 + len(REPEATED)))
            for k in range(STEPS):
                nc.scalar.copy(w_dots_hi[:, k, :], w_dots[:, k, :]).then_inc(w_hi_ready, 1)
            act.wait_ge(dots_zeroed, 1)
            act.wait_ge(hotT_ready, HOT - 1)
            feats_hot(hotT[:, :, 0, :], range(HOT - 1))
            act.wait_ge(onehot_used, blocks_to(HOT))
            feats_hot(hot_sum[(HOT - 1) % 2].rearrange("d (i b) -> d i b", b=P)[:, 0:1], range(HOT - 1, HOT)
                      ).then_inc(tile_hot, 1)
            hot_out(HOT - 1)
            act.wait_ge(wsum_ready, 1)
            nc.scalar.copy(w_dsum_hi[:, :], w_dsum[:, :]).then_inc(w_hi_ready, 1)
            for c in range(CHUNKS):
                spread_chunk(0, c)
            dots_upper(0)
            act.wait_ge(small_loaded, 16 * 4)
            act.wait_ge(hotT_ready, HOT)
            with act.Fori(1, TILES) as t:
                act.wait_ge(gram_done, CHUNKS * t)
                feats(t, 1)
                hot_tile(t)
                for j in range(3, GROUPS, 2):
                    feats(t, j)
                act.wait_ge(dots_lo_ready, STEPS * t)
                for c in range(CHUNKS):
                    spread_chunk(t, c)
                    if c == 1:
                        h1_relu(t - 1)
                act.wait_ge(l1_done, t)
                dots_upper(t)
            for n, k in enumerate(range(0, K2, 2)):
                act.wait_ge(last_turned_act, n + 1)
                nc.scalar.activation(h1T[:, k, :], last_turned[k], ACT.Relu, bias=b1_col[:, k:k + 1]).then_inc(
                    last_h1T_act, 1)

        @block.vector
        def _(dve):
            def hot_lower(i):
                if i >= 2:
                    dve.wait_ge(onehot_used, blocks_to(i - 1))
                for a, b in HALVES if i == 0 else [(0, BLOCKS[i])]:
                    dve.wait_ge(hi_ready, parts_of(i, a))
                    nc.vector.tensor_sub(hot_lo[i % 2][:, a:b, :], hot_rows[:, i % ROW_BUFFERS, a:b, :],
                                         hot_hi[i % 2][:, a:b, :].bitcast(FP32)).then_inc(lo_ready, 1)
                    if (i, a) == (0, 0):
                        hot_onehots(0, range(0, AHEAD))

            def hot_onehots(i, blocks):
                dve.wait_ge(hot_ids_loaded[i], 16)
                for c in blocks:
                    n = vec_to(i, c)
                    if n >= ONES:
                        user, block = (i, c - ONES) if c >= ONES else (i - 1, VEC_BLOCKS[i - 1] + c - ONES)
                        dve.wait_ge(onehot_used, blocks_to(user, block + 1))
                    nc.vector.tensor_scalar(onehot[n % ONES][:, :], hot_ids_all[:, i, :],
                                            row_no[:, LAYOUTS.index(BLOCKS[i]), c:c + 1], None,
                                            op0=ALU.is_equal).then_inc(onehot_ready, 1)

            def dense_of(t):
                return denseT[:, bass.ds(t, 1), :].rearrange("d t b -> d (t b)")

            def dense_feat(t):
                nc.vector.tensor_copy(featT[:, :, 0], dense_of(t)).then_inc(tile_dense, 1)

            def dense_parts(t):
                nc.vector.tensor_copy(dense_hi[:, :], dense_of(t)).then_inc(dense_hi_ready, 1)
                dve.wait_ge(dense_hi_ready, t + 1)
                nc.vector.tensor_sub(dense_lo[:, :], dense_of(t), dense_hi[:, :].bitcast(FP32)).then_inc(
                    dense_parts_ready, 1)

            def feats(t, j):
                dve.wait_ge(turned_done, GROUPS * t + j + 1)
                for i, f, n in runs(MEMBERS[j]):
                    last = nc.vector.tensor_copy(featT_by_feat[:, 1 + f:1 + f + n], turned[0][:, i:i + n, :])
                last.then_inc(feat_vec, 1)

            def spread_chunk(t, c, more=True):
                dve.wait_ge(gram_done, CHUNKS * t + c + 1)
                if c == CHUNKS - 1 and more:
                    feats(t + 1, 0)
                spread(dve, nc.vector.tensor_copy, (0, 1), t, c, spare_vec).then_inc(dots_vec, 1)

            def dots_lower(t):
                for k in range(STEPS):
                    dve.wait_ge(dots_hi_ready, STEPS * t + k + 1)
                    nc.vector.tensor_sub(dots_lo[:, k, :], dots[:, k, :], dots_hi[:, k, :].bitcast(FP32)
                                         ).then_inc(dots_lo_ready, 1)

            def add_lone(t, layer_sum, cols):
                dve.wait_ge(lone_ready, t + 1)
                return nc.vector.scalar_tensor_tensor(h1[:, cols], w_lone[:, cols], lone_dot[:, :], layer_sum,
                                                      op0=ALU.mult, op1=ALU.add)

            def h1_copy(t):
                dve.wait_ge(l1_done, t + 1)
                add_lone(t, layer[:, :], slice(0, H1)).then_inc(h1_ready, 1)

            def lone_pair(t):
                dve.wait_ge(turned_done, GROUPS * (t + 1))
                if not (isinstance(t, int) and t == 0):
                    dve.wait_ge(h1_ready, t)
                y, z = (rows[:, f - 1, :] for f in LONE_PAIR)
                nc.vector.scalar_tensor_tensor(lone_product[:, :], y, 1.0, z, op0=ALU.mult, op1=ALU.mult,
                                               accum_out=lone_dot[:, :]).then_inc(lone_ready, 1)

            def last_layer(t):
                dve.wait_ge(l2_done, t + 1)
                nc.vector.tensor_add(h2[:, :], layer2, b2_all[:, :]).then_inc(h2_ready, 1)
                dve.wait_ge(h2_ready, t + 1)
                nc.vector.scalar_tensor_tensor(h2w[:, :], h2[:, :], 0.0, w3_all[:, :], op0=ALU.max, op1=ALU.mult,
                                               accum_out=y_now[:, :]).then_inc(y_ready, 1)
                dve.wait_ge(y_ready, t + 1)
                nc.vector.tensor_copy(y_all[:, bass.ds(t, 1)], y_now[:, :]).then_inc(y_stored, 1)

            def collect(t):
                for j in range(4, GROUPS, 2):
                    feats(t, j)
                h1_copy(t - 1)
                dense_parts(t)
                lone_pair(t)

            def w_lower(k):
                dve.wait_ge(w_hi_ready, k + 1)
                nc.vector.tensor_sub(w_dots_lo[:, k, :], w_dots[:, k, :], w_dots_hi[:, k, :].bitcast(FP32)
                                     ).then_inc(w_lo_ready, 1)

            nc.vector.memset(w_dots[:, :, :], 0.0).then_inc(w_zeroed, 1)
            nc.vector.memset(dots[:, :, :], 0.0).then_inc(dots_zeroed, 1)
            nc.vector.memset(ones_row[:, :], 1.0).then_inc(ones_made, 1)
            dve.wait_ge(row_no_made, len(LAYOUTS))
            nc.vector.tensor_copy(row_no[:, :, :], row_no_int[:, :, :]).then_inc(row_no_ready, 1)
            nc.vector.tensor_scalar(row_no_neg[:, :, :], row_no_int[:, :, :], -1.0, None, op0=ALU.mult).then_inc(
                row_no_ready, 1)
            dve.wait_ge(row_no_ready, 1)
            hot_lower(0)
            hot_onehots(0, range(AHEAD, VEC_BLOCKS[0]))
            for i in range(1, HOT):
                hot_lower(i)
                hot_onehots(i, range(0, AHEAD))
                for j in first_tile_groups(i):
                    if j % 2 == 0:
                        feats(0, j)
                hot_onehots(i, range(AHEAD, VEC_BLOCKS[i]))
            dve.wait_ge(denseT_ready, 1)
            dense_feat(0)
            dense_parts(0)
            lone_pair(0)
            dve.wait_ge(wd_loaded, 32)
            nc.vector.tensor_add(w_dsum[:, :], w_dense[:, 0, :], w_dense[:, 1, :]).then_inc(wsum_ready, 1)
            for k in range(W_FIRST):
                w_lower(k)
            dve.wait_ge(w_hi_ready, STEPS + 1)
            nc.vector.tensor_sub(w_dsum_lo[:, :], w_dsum[:, :], w_dsum_hi[:, :].bitcast(FP32)).then_inc(w_lo_ready, 1)
            dve.wait_ge(small_loaded, 16 * 4)
            dve.wait_ge(dots_zeroed, 1)
            for c in range(CHUNKS):
                spread_chunk(0, c)
                if W_FIRST + c < STEPS:
                    w_lower(W_FIRST + c)
            dots_lower(0)
            dense_feat(1)
            feats(1, 2)
            collect(1)
            with dve.Fori(1, TILES - 1) as t:
                for c in range(CHUNKS):
                    spread_chunk(t, c)
                dots_lower(t)
                dense_feat(t + 1)
                feats(t + 1, 2)
                last_layer(t - 1)
                collect(t + 1)
            for c in range(CHUNKS):
                spread_chunk(TILES - 1, c, more=False)
            dots_lower(TILES - 1)
            last_layer(TILES - 2)
            for h, layer_sum in enumerate(last_halves):
                dve.wait_ge(last_half_done, h + 1)
                add_lone(TILES - 1, layer_sum, slice(H1 // 2 * h, H1 // 2 * (h + 1))).then_inc(last_half_ready, 1)
            for n, k in enumerate(range(1, K2, 2)):
                dve.wait_ge(last_turned_vec, n + 1)
                nc.vector.tensor_scalar(h1T[:, k, :], last_turned[k], b1_col[:, k:k + 1], 0.0, op0=ALU.add,
                                        op1=ALU.max).then_inc(last_h1T_vec, 1)
            dve.wait_ge(last_sum_done, 1)
            nc.vector.scalar_tensor_tensor(h2w[:, :], last_layer2, 0.0, w3_all[:, :], op0=ALU.max, op1=ALU.mult,
                                           accum_out=y_all[:, TILES - 1:TILES]).then_inc(y_stored, 1)


def kernel(**inputs):
    import concourse.bacc as bacc
    from concourse.bass_utils import run_bass_kernel_spmd

    nc = bacc.Bacc("TRN2", target_bir_lowering=False, num_devices=1)
    arrays = {}

    def given(name):
        a = np.ascontiguousarray(inputs[name])
        arrays[f"in_{name}"] = a
        return nc.dram_tensor(f"in_{name}", a.shape, mybir.dt.from_np(a.dtype), kind="ExternalInput").ap()

    ids = given("ids")
    hot = np.asarray(inputs["ids"])[:, HOT_TABLES].reshape(P, TILES, HOT).transpose(2, 1, 0)
    arrays["in_hot_ids"] = np.ascontiguousarray(hot).reshape(HOT, BATCH)
    hot_ids = nc.dram_tensor("in_hot_ids", (HOT, BATCH), mybir.dt.from_np(arrays["in_hot_ids"].dtype),
                             kind="ExternalInput").ap()
    tables = [given(f"tbl_{f}") for f in range(TABLES)]
    dense, w1, b1, w2, b2, w3 = (given(n) for n in ("r_dense_features", "W_top1", "b_top1", "W_top2", "b_top2",
                                                    "W_top3"))
    out = nc.dram_tensor("out", (BATCH, 1), FP32, kind="ExternalOutput").ap()
    build(nc, ids, hot_ids, tables, dense, w1, b1, w2, b2, w3, out)
    return run_bass_kernel_spmd(nc, [arrays], core_ids=[0]).results[0]["out"]
```
